# Optimizing a Trainium2 kernel written in Bass

```python
import numpy as np
import jax
import jax.numpy as jnp

def _softmax(x, axis=-1):
    return jax.nn.softmax(x, axis=axis)

def _gelu(x):
    return jax.nn.gelu(x, approximate=True)

def _silu(x):
    return jax.nn.silu(x)

def _sigmoid(x):
    return jax.nn.sigmoid(x)

def _layernorm(x, axis=-1, eps=1e-05):
    m = jnp.mean(x, axis=axis, keepdims=True)
    v = jnp.var(x, axis=axis, keepdims=True)
    return (x - m) / jnp.sqrt(v + eps)

def _scatter_add(tgt, idx, src, axis=0):
    return tgt.at[idx].add(src)

def _segment_sum(src, seg, n):
    return jax.ops.segment_sum(src, seg, n)
kernel_name = 'mk_gnn_preln_d4_gnn_r8_213cca'

def setup_inputs(seed: int=0):
    np.random.seed(seed)
    _w = jnp.asarray

    def _rec_inputs():
        import jax
        import jax.numpy as jnp
        _gk = jax.random.key(seed)
        x = -8.776e-05 + 1 * jax.random.normal(jax.random.fold_in(_gk, 1), (1250, 512), jnp.float32)
        src = jax.random.randint(jax.random.fold_in(_gk, 2), (20000,), 0, 1250, jnp.int32)
        dst = jnp.minimum((1250 * jax.random.uniform(jax.random.fold_in(_gk, 3), (20000,)) ** 2.0).astype(jnp.int32), 9999)
        _o = jnp.argsort(dst, stable=True)
        src = src[_o]
        dst = dst[_o]
        return (x, src, dst)
    x, src, dst = _rec_inputs()

    def _L0_gnn_setup():
        import jax, jax.numpy as jnp
        import numpy as np
        N_NODES = 1250
        key = jax.random.key(seed)
        k1, k2, k3, k4, k5 = jax.random.split(key, 5)
        x = jax.random.normal(k1, (N_NODES, 512), dtype=jnp.float32)
        edge_index = jax.random.randint(k2, (2, 20000), 0, N_NODES, dtype=jnp.int64)
        W_l = jax.random.normal(k3, (512, 512), dtype=jnp.float32) * 0.04
        b_l = jax.random.normal(k4, (512,), dtype=jnp.float32) * 0.04
        W_r = jax.random.normal(k5, (512, 512), dtype=jnp.float32) * 0.04
        return {'x': x, 'edge_index': edge_index, 'W_l': W_l, 'b_l': b_l, 'W_r': W_r}
    _L0_gnn_all = _L0_gnn_setup()
    _L0_gnn_in = {k: v for k, v in _L0_gnn_all.items() if k in ('W_l', 'b_l', 'W_r')}
    del _L0_gnn_all

    def _L1_gnn_setup():
        import jax, jax.numpy as jnp
        import numpy as np
        N = 6250
        E = 50000
        D = 512

        def _sage(x, src, dst, Wl, b, Wr):
            n = x.shape[0]
            msgs = x[src]
            summed = jax.ops.segment_sum(msgs, dst, num_segments=n)
            cnt = jax.ops.segment_sum(jnp.ones((src.shape[0],), x.dtype), dst, num_segments=n)
            mean = summed / jnp.maximum(cnt, 1.0)[:, None]
            return mean @ Wl + b + x @ Wr
        key = jax.random.key(seed)
        ks = jax.random.split(key, 8)
        s = 1.0 / np.sqrt(D)
        x = jax.random.normal(ks[0], (N, D), dtype=jnp.float32)
        edge_index = jax.random.randint(ks[1], (2, E), 0, N, dtype=jnp.int64)
        W1l = jax.random.uniform(ks[2], (D, D), jnp.float32, -s, s)
        b1 = jax.random.uniform(ks[3], (D,), jnp.float32, -s, s)
        W1r = jax.random.uniform(ks[4], (D, D), jnp.float32, -s, s)
        W2l = jax.random.uniform(ks[5], (D, D), jnp.float32, -s, s)
        b2 = jax.random.uniform(ks[6], (D,), jnp.float32, -s, s)
        W2r = jax.random.uniform(ks[7], (D, D), jnp.float32, -s, s)
        return {'x': x, 'edge_index': edge_index, 'W1l': W1l, 'b1': b1, 'W1r': W1r, 'W2l': W2l, 'b2': b2, 'W2r': W2r}
    _L1_gnn_all = _L1_gnn_setup()
    _L1_gnn_in = {k: v for k, v in _L1_gnn_all.items() if k in ('W1l', 'b1', 'W1r', 'W2l', 'b2', 'W2r')}
    del _L1_gnn_all

    def _L2_gnn_setup():
        import jax, jax.numpy as jnp
        import numpy as np
        N_NODES = 1250
        N_EDGES = 20000
        DIM = 512
        LN_EPS = 1e-05
        key = jax.random.key(seed)
        ks = jax.random.split(key, 6)
        scale = 1.0 / np.sqrt(DIM)
        h = jax.random.normal(ks[0], (N_NODES, DIM), dtype=jnp.float32)
        edge_index = jax.random.randint(ks[1], (2, N_EDGES), 0, N_NODES, dtype=jnp.int32)
        W_self = jax.random.normal(ks[2], (DIM, DIM), dtype=jnp.float32) * scale
        b_self = jnp.zeros((DIM,), dtype=jnp.float32)
        W_neigh = jax.random.normal(ks[3], (DIM, DIM), dtype=jnp.float32) * scale
        b_neigh = jnp.zeros((DIM,), dtype=jnp.float32)
        ln_gamma = jnp.ones((DIM,), dtype=jnp.float32)
        ln_beta = jnp.zeros((DIM,), dtype=jnp.float32)
        return {'h': h, 'edge_index': edge_index, 'W_self': W_self, 'b_self': b_self, 'W_neigh': W_neigh, 'b_neigh': b_neigh, 'ln_gamma': ln_gamma, 'ln_beta': ln_beta}
    _L2_gnn_all = _L2_gnn_setup()
    _L2_gnn_in = {k: v for k, v in _L2_gnn_all.items() if k in ('W_self', 'b_self', 'W_neigh', 'b_neigh', 'ln_gamma', 'ln_beta')}
    del _L2_gnn_all

    def _L3_gnn_setup():
        import jax, jax.numpy as jnp
        import numpy as np
        N, E, D = (6250, 18750, 512)

        def _gcn_conv(x, src, dst, W, b, n):
            h = x @ W
            deg = jax.ops.segment_sum(jnp.ones_like(dst, dtype=x.dtype), dst, num_segments=n)
            dis = jnp.where(deg > 0, jax.lax.rsqrt(jnp.maximum(deg, 1.0)), 0.0)
            norm = dis[src] * dis[dst]
            msg = h[src] * norm[:, None]
            out = jax.ops.segment_sum(msg, dst, num_segments=n)
            return out + b
        key = jax.random.key(seed)
        k = jax.random.split(key, 6)
        x = jax.random.normal(k[0], (N, D), dtype=jnp.float32)
        edge_index = jax.random.randint(k[1], (2, E), 0, N, dtype=jnp.int64)
        s = 1.0 / np.sqrt(D)
        W1 = jax.random.uniform(k[2], (D, D), dtype=jnp.float32, minval=-s, maxval=s)
        b1 = jnp.zeros((D,), dtype=jnp.float32)
        W2 = jax.random.uniform(k[3], (D, D), dtype=jnp.float32, minval=-s, maxval=s)
        b2 = jnp.zeros((D,), dtype=jnp.float32)
        return {'x': x, 'edge_index': edge_index, 'W1': W1, 'b1': b1, 'W2': W2, 'b2': b2}
    _L3_gnn_all = _L3_gnn_setup()
    _L3_gnn_in = {k: v for k, v in _L3_gnn_all.items() if k in ('W1', 'b1', 'W2', 'b2')}
    del _L3_gnn_all
    return {'x': x, 'src': src, 'dst': dst, 'L0_gnn_W_l': _L0_gnn_in['W_l'], 'L0_gnn_b_l': _L0_gnn_in['b_l'], 'L0_gnn_W_r': _L0_gnn_in['W_r'], 'L1_gnn_W1l': _L1_gnn_in['W1l'], 'L1_gnn_b1': _L1_gnn_in['b1'], 'L1_gnn_W1r': _L1_gnn_in['W1r'], 'L1_gnn_W2l': _L1_gnn_in['W2l'], 'L1_gnn_b2': _L1_gnn_in['b2'], 'L1_gnn_W2r': _L1_gnn_in['W2r'], 'L2_gnn_W_self': _L2_gnn_in['W_self'], 'L2_gnn_b_self': _L2_gnn_in['b_self'], 'L2_gnn_W_neigh': _L2_gnn_in['W_neigh'], 'L2_gnn_b_neigh': _L2_gnn_in['b_neigh'], 'L2_gnn_ln_gamma': _L2_gnn_in['ln_gamma'], 'L2_gnn_ln_beta': _L2_gnn_in['ln_beta'], 'L3_gnn_W1': _L3_gnn_in['W1'], 'L3_gnn_b1': _L3_gnn_in['b1'], 'L3_gnn_W2': _L3_gnn_in['W2'], 'L3_gnn_b2': _L3_gnn_in['b2']}

def reference(x, src, dst, L0_gnn_W_l, L0_gnn_b_l, L0_gnn_W_r, L1_gnn_W1l, L1_gnn_b1, L1_gnn_W1r, L1_gnn_W2l, L1_gnn_b2, L1_gnn_W2r, L2_gnn_W_self, L2_gnn_b_self, L2_gnn_W_neigh, L2_gnn_b_neigh, L2_gnn_ln_gamma, L2_gnn_ln_beta, L3_gnn_W1, L3_gnn_b1, L3_gnn_W2, L3_gnn_b2):
    import jax
    import jax.numpy as jnp

    def _L0_gnn_ref(x, edge_index, W_l, b_l, W_r):
        import jax, jax.numpy as jnp
        import numpy as np
        N_NODES = 1250
        src, dst = (edge_index[0], edge_index[1])
        n = x.shape[0]
        summed = jax.ops.segment_sum(x[src], dst, num_segments=n)
        deg = jax.ops.segment_sum(jnp.ones_like(src, dtype=x.dtype), dst, num_segments=n)
        agg = summed / jnp.maximum(deg, 1.0)[:, None]
        out = agg @ W_l.T + b_l + x @ W_r.T
        out = jax.nn.relu(out)
        return out

    def _L1_gnn_ref(x, edge_index, W1l, b1, W1r, W2l, b2, W2r):
        import jax, jax.numpy as jnp
        import numpy as np
        N = 6250
        E = 50000
        D = 512

        def _sage(x, src, dst, Wl, b, Wr):
            n = x.shape[0]
            msgs = x[src]
            summed = jax.ops.segment_sum(msgs, dst, num_segments=n)
            cnt = jax.ops.segment_sum(jnp.ones((src.shape[0],), x.dtype), dst, num_segments=n)
            mean = summed / jnp.maximum(cnt, 1.0)[:, None]
            return mean @ Wl + b + x @ Wr
        src, dst = (edge_index[0], edge_index[1])
        h = jax.nn.relu(_sage(x, src, dst, W1l, b1, W1r))
        return _sage(h, src, dst, W2l, b2, W2r)

    def _L2_gnn_ref(h, edge_index, W_self, b_self, W_neigh, b_neigh, ln_gamma, ln_beta):
        import jax, jax.numpy as jnp
        import numpy as np
        N_NODES = 1250
        N_EDGES = 20000
        DIM = 512
        LN_EPS = 1e-05
        n = h.shape[0]
        src = edge_index[0]
        dst = edge_index[1]
        msg = h[dst] @ W_neigh.T + b_neigh
        neigh = jax.ops.segment_sum(msg, src, num_segments=n)
        deg = jax.ops.segment_sum(jnp.ones(src.shape, h.dtype), src, num_segments=n)
        deg = jnp.maximum(deg, 1.0)
        neigh = neigh / deg[:, None]
        out = jax.nn.relu(h @ W_self.T + b_self + neigh)
        x = h + out
        mean = jnp.mean(x, axis=-1, keepdims=True)
        var = jnp.mean(jnp.square(x - mean), axis=-1, keepdims=True)
        return (x - mean) * jax.lax.rsqrt(var + LN_EPS) * ln_gamma + ln_beta

    def _L3_gnn_ref(x, edge_index, W1, b1, W2, b2):
        import jax, jax.numpy as jnp
        import numpy as np
        N, E, D = (6250, 18750, 512)

        def _gcn_conv(x, src, dst, W, b, n):
            h = x @ W
            deg = jax.ops.segment_sum(jnp.ones_like(dst, dtype=x.dtype), dst, num_segments=n)
            dis = jnp.where(deg > 0, jax.lax.rsqrt(jnp.maximum(deg, 1.0)), 0.0)
            norm = dis[src] * dis[dst]
            msg = h[src] * norm[:, None]
            out = jax.ops.segment_sum(msg, dst, num_segments=n)
            return out + b
        n = x.shape[0]
        loops = jnp.arange(n, dtype=edge_index.dtype)
        src = jnp.concatenate([edge_index[0], loops])
        dst = jnp.concatenate([edge_index[1], loops])
        h = _gcn_conv(x, src, dst, W1, b1, n)
        h = jax.nn.relu(h)
        return _gcn_conv(h, src, dst, W2, b2, n)
    edge_index = jnp.stack([src, dst])
    h = jnp.maximum(_layernorm(x, axis=-1), 0.0)
    x = x + _L0_gnn_ref(h, edge_index, L0_gnn_W_l, L0_gnn_b_l, L0_gnn_W_r)
    h = jnp.maximum(_layernorm(x, axis=-1), 0.0)
    x = x + _L1_gnn_ref(h, edge_index, L1_gnn_W1l, L1_gnn_b1, L1_gnn_W1r, L1_gnn_W2l, L1_gnn_b2, L1_gnn_W2r)
    h = jnp.maximum(_layernorm(x, axis=-1), 0.0)
    x = x + _L2_gnn_ref(h, edge_index, L2_gnn_W_self, L2_gnn_b_self, L2_gnn_W_neigh, L2_gnn_b_neigh, L2_gnn_ln_gamma, L2_gnn_ln_beta)
    h = jnp.maximum(_layernorm(x, axis=-1), 0.0)
    x = x + _L3_gnn_ref(h, edge_index, L3_gnn_W1, L3_gnn_b1, L3_gnn_W2, L3_gnn_b2)
    return x

_drawn_inputs = setup_inputs


def setup_inputs(seed=0):
    import zlib

    import numpy as np

    out = dict(_drawn_inputs(seed))
    spreads = {'L2_gnn_b_self': (0.0, 0.1),
     'L2_gnn_b_neigh': (0.0, 0.1),
     'L2_gnn_ln_gamma': (1.0, 0.2),
     'L2_gnn_ln_beta': (0.0, 0.1),
     'L3_gnn_b1': (0.0, 0.335),
     'L3_gnn_b2': (0.0, 0.1)}
    factors = {'L1_gnn_b1': 4.578}
    for name, (base, spread) in spreads.items():
        noise = np.random.default_rng([zlib.crc32(name.encode()), seed]).standard_normal(out[name].shape)
        drawn = base * np.exp(spread * noise) if base else spread * noise
        out[name] = jnp.asarray(drawn.astype(out[name].dtype))
    for name, factor in factors.items():
        out[name] = (out[name] * factor).astype(out[name].dtype)
    return out
```

```python
import concourse.bass as bass
from concourse import mybir

F32 = mybir.dt.float32
F32R = mybir.dt.float32r
BF16 = mybir.dt.bfloat16
FP16 = mybir.dt.float16
I32 = mybir.dt.int32
U16 = mybir.dt.uint16
ALU = mybir.AluOpType
ACT = mybir.ActivationFunctionType
AX_X = mybir.AxisListType.X

P = 128
EPS = 1e-5
EXACT = 4096.0
NOWHERE = 4000

CONVS = [
    dict(neigh="L0_gnn_W_l", own="L0_gnn_W_r", bias="L0_gnn_b_l", turned=True, source="x", by="dst"),
    dict(neigh="L1_gnn_W1l", own="L1_gnn_W1r", bias="L1_gnn_b1", turned=False, source="x", by="dst"),
    dict(neigh="L1_gnn_W2l", own="L1_gnn_W2r", bias="L1_gnn_b2", turned=False, source="hidden", by="dst"),
    dict(neigh="L2_gnn_W_neigh", own="L2_gnn_W_self", bias="L2_gnn_b_self", turned=True, source="x", by="src"),
    dict(neigh="L3_gnn_W1", own=None, bias="L3_gnn_b1", turned=False, source="x", by="dst"),
    dict(neigh="L3_gnn_W2", own=None, bias="L3_gnn_b2", turned=False, source="hidden", by="dst"),
]
L0, L1A, L1B, L2, L3A, L3B = range(6)
NEW_X = {L0: 0, L1B: 1, L2: 2, L3B: 3}
NORMED = {L0: 0, L1A: 1, L2: 2, L3A: 3}


def gnn_kernel(nc, ins, out):
    x_dram, src_dram, dst_dram = ins["x"], ins["src"], ins["dst"]
    N, D = x_dram.shape
    E = src_dram.shape[0]
    NT = (N + P - 1) // P
    NP = NT * P
    LAST = N - (NT - 1) * P
    KF = D // P
    ET = (E + P - 1) // P
    UNITS = (ET + 1) // 2
    ETP = 2 * UNITS
    FULL, REST = E // P, E % P
    RING = 4
    assert D == 512 and NT % 2 == 0 and P < FULL < ETP <= 2 * P and LAST > 96

    weights = []
    for s, c in enumerate(CONVS):
        for slot, name in enumerate([c["neigh"], c["own"]]):
            if name:
                weights.append((s, slot, name, c["turned"], sum(w[3] for w in weights)))

    def weights_of(s, slot=None):
        return [n for n, w in enumerate(weights) if w[0] == s and slot in (None, w[1])]

    at = [(nc.sbuf_base + 31) // 32 * 32]

    def place(name, shape, dtype, where=None):
        size = mybir.dt.size(dtype)
        for d in shape[1:]:
            size *= d
        if where is None:
            where = at[0]
            at[0] += (size + 31) // 32 * 32
        place.end = where + (size + 31) // 32 * 32
        return nc.alloc_sbuf_tensor_at(name, list(shape), dtype, offset=where), where

    count16, _ = place("count16", [P, NT, NP], U16)
    countT16, _ = place("countT16", [P, NT, NP], U16)
    cstage, _ = place("cstage", [P, 2, NT, P], F32R)
    x, _ = place("x", [P, NT, D], F32)
    p_hi, p_at = place("p_hi", [P, NT, D], F32R)
    p_lo, _ = place("p_lo", [P, NT, D], F32R)
    own, own_at = place("own", [P, NT, D], F32)
    w_hi, _ = place("w_hi", [P, 2, KF, D], F32R)
    w_lo, _ = place("w_lo", [P, 2, KF, D], F32R)
    wstage, _ = place("wstage", [P, KF, D], F32)
    z, z_at = place("z", [P, 2, D], F32)
    hT_hi, _ = place("hT_hi", [P, 2, KF, P], F32R)
    hT_lo, _ = place("hT_lo", [P, 2, KF, P], F32R)
    vec, _ = place("vec", [P, 5, D], F32)
    mix2, _ = place("mix2", [P, D], F32)
    exact, _ = place("exact", [P, P], F32)
    ident, _ = place("ident", [P, P], F32)
    stats, _ = place("stats", [P, 6], F32)
    mv_now, _ = place("mv_now", [P, 2], F32)
    mv, _ = place("mv", [P, NT, 2], F32)
    std, _ = place("std", [P, NT], F32)
    rstd, _ = place("rstd", [P, NT], F32)
    deg_in, _ = place("deg_in", [P, NT], F32)
    deg_out, _ = place("deg_out", [P, NT], F32)
    inv_in, _ = place("inv_in", [P, NT], F32)
    inv_out, _ = place("inv_out", [P, NT], F32)
    has_out, _ = place("has_out", [P, NT], F32)
    dis, _ = place("dis", [P, NT], F32)
    dis2, _ = place("dis2", [P, NT], F32)
    imv, _ = place("imv", [P, 4], F32)
    eps, _ = place("eps", [P, 1], F32)
    big_i, _ = place("big_i", [1, 1], I32)
    junk, _ = place("junk", [P, NP], BF16, z_at)
    iota, _ = place("iota", [P, NP], FP16, p_at)
    src_hot, _ = place("src_hot", [P, RING, 2, NP], BF16, place.end)
    dst_hot, _ = place("dst_hot", [P, RING, 2, P], BF16, place.end)
    cblock, _ = place("cblock", [P, 2, NP], F32, place.end)
    zeros, _ = place("zeros", [P, D], BF16, place.end)
    assert place.end <= own_at
    e_int, _ = place("e_int", [P, 2, 2, P], I32, own_at)
    e_f, _ = place("e_f", [P, 2, 2, P], F32, place.end)
    nodeT, _ = place("nodeT", [P, 2, ETP], F32, place.end)
    reach, _ = place("reach", [P, 4], F32, place.end)
    reachB, _ = place("reachB", [P, 4, NT], F32, place.end)
    block_lo, _ = place("block_lo", [P, 1], F32, place.end)
    block_hi, _ = place("block_hi", [P, 1], F32, place.end)
    unit_up, _ = place("unit_up", [P, ETP], F32, place.end)
    unit_dn, _ = place("unit_dn", [P, ETP], F32, place.end)
    hit, _ = place("hit", [P, ETP], F32, place.end)
    marks, _ = place("marks", [P, 2, ETP], F32, place.end)
    ends, _ = place("ends", [P, 2], F32, place.end)
    low, _ = place("low", [P, 1], F32, place.end)
    length, _ = place("length", [P, 1], F32, place.end)
    span, _ = place("span", [P, 2], F32, place.end)
    before, _ = place("before", [P, NT + 1], F32, place.end)
    starts, _ = place("starts", [1, 16], F32, place.end)
    starts_i, _ = place("starts_i", [1, 16], I32, place.end)
    shift_i, _ = place("shift_i", [1, 16], I32, place.end)
    top, _ = place("top", [P, 1], F32, place.end)
    top1, _ = place("top1", [1, 1], F32, place.end)
    assert place.end <= own_at + NT * D * 4
    assert at[0] <= nc.sbuf_usable_end, (at[0], nc.sbuf_usable_end)
    ps = nc.alloc_psum_tensor("ps", [P, 8, 512], F32)
    HT, PP, QQ, AGG = 0, 2, 4, 6

    sems = {}

    def sem(name):
        if name not in sems:
            sems[name] = nc.alloc_semaphore(name)
        return sems[name]

    def tile(s, i):
        return NT * s + i + 1 + 2

    z_ready, zT_ready, hi_done, lo_done = sem("z_ready"), sem("zT_ready"), sem("hi_done"), sem("lo_done")
    p_ready, phi_done, plo_done = sem("p_ready"), sem("phi_done"), sem("plo_done")
    q_ready, q_half, q_done = sem("q_ready"), sem("q_half"), sem("q_done")
    stage_ready, agg_ready, t_done, x_done = sem("stage_ready"), sem("agg_ready"), sem("t_done"), sem("x_done")
    stats_done, mv_done, std_done, rstd_done = sem("stats_done"), sem("mv_done"), sem("std_done"), sem("rstd_done")
    w_loaded, wT_ready, whi_done, wlo_done = sem("w_loaded"), sem("wT_ready"), sem("whi_done"), sem("wlo_done")
    hot_ready, hot_used = sem("hot_ready"), sem("hot_used")
    counts_ready, counts_out, cT_ready, cT_out, c16_done = (
        sem("counts_ready"), sem("counts_out"), sem("cT_ready"), sem("cT_out"), sem("c16_done"))
    vec_loaded = [sem(f"vec{k}_loaded") for k in range(5)]
    dst_loaded, src_loaded, x_loaded = sem("dst_loaded"), sem("src_loaded"), sem("x_loaded")
    pads_set, x_pad_set, pool_consts, dve_consts = sem("pads_set"), sem("x_pad_set"), sem("pool_consts"), sem("dve_consts")
    ident0, before0 = sem("ident0"), sem("before0")
    table_step, table_pe = sem("table_step"), sem("table_pe")
    scale_step, scale_act = sem("scale_step"), sem("scale_act")
    top_turned, big_ready, deg_out_done = sem("top_turned"), sem("big_ready"), sem("deg_out_done")
    l2_step, l2_std, l2_t, l2_w, l2_xb, l2_scaled = (
        sem("l2_step"), sem("l2_std"), sem("l2_t"), sem("l2_w"), sem("l2_xb"), sem("l2_scaled"))
    coarse_set, exact_set, fine_set = sem("coarse_set"), sem("exact_set"), sem("fine_set")
    aggr_done = sem("aggr_done")
    passed_dve, passed_pool = sem("passed_dve"), sem("passed_pool")
    out_stored = sem("out_stored")

    VSLOT = {L0: 0, L1A: 1, L1B: 0, L2: 1, L3A: 0, L3B: 1}
    VCOUNT = {L0: 16, L1A: 16, L1B: 32, L2: 32, L3A: 48, L3B: 48}
    BNEIGH, GAMMA, BETA = 2, 3, 4

    def mm_done(engine, s, i):
        engine.wait_ge(q_ready if CONVS[s]["own"] else p_ready, tile(s, i))

    def dma_rows(engine, dram, sbuf, sem_, store=False):
        whole, rest = dram[0:(NT - 1) * P, :].rearrange("(t p) d -> p t d", p=P), dram[(NT - 1) * P:N, :]
        for a, b in ((sbuf[:, 0:NT - 1, :], whole), (sbuf[0:LAST, NT - 1, :], rest)):
            engine.dma_start(b if store else a, a if store else b).then_inc(sem_, 16)

    def row_of(name):
        return ins[name].partition_broadcast(P)

    with nc.Block() as block:

        @block.sync
        def _(sp):
            sp.wait_ge(pads_set, 1)
            for k, (dram, s_) in enumerate(((dst_dram, dst_loaded), (src_dram, src_loaded))):
                sp.dma_start(e_int[:, k, 0, :], dram[0:P * P].rearrange("(t e) -> t e", e=P)).then_inc(s_, 16)
                sp.dma_start(e_int[0:FULL - P, k, 1, :],
                             dram[P * P:FULL * P].rearrange("(t e) -> t e", e=P)).then_inc(s_, 16)
                if REST:
                    sp.dma_start(e_int[FULL - P:FULL - P + 1, k, 1, 0:REST],
                                 dram[FULL * P:E].rearrange("(t e) -> t e", t=1)).then_inc(s_, 16)
            sp.wait_ge(x_pad_set, 1)
            dma_rows(sp, x_dram, x, x_loaded)
            rows = [(VSLOT[L0], CONVS[L0]["bias"], None), (VSLOT[L1A], CONVS[L1A]["bias"], None),
                    (BNEIGH, "L2_gnn_b_neigh", None), (GAMMA, "L2_gnn_ln_gamma", None), (BETA, "L2_gnn_ln_beta", None)]
            rows += [(VSLOT[s], CONVS[s]["bias"], s - 2) for s in (L1B, L2, L3A, L3B)]
            loads = [("w", n) for n in range(len(weights))]
            order = loads[:1] + [("v", r) for r in rows[:5]] + loads[1:5]
            order += [("v", rows[5])] + loads[5:6] + [("v", rows[6])] + loads[6:8]
            order += [("v", rows[7])] + loads[8:9] + [("v", rows[8])] + loads[9:]
            for kind, what in order:
                if kind == "w":
                    if what:
                        sp.wait_ge(wlo_done, KF * what)
                    sp.dma_start(wstage[:, :, :],
                                 ins[weights[what][2]].rearrange("(k p) f -> p k f", p=P)).then_inc(w_loaded, 16)
                else:
                    slot, name, after = what
                    if after is not None:
                        sp.wait_ge(q_done, tile(after, NT - 1))
                    sp.dma_start(vec[:, slot, :], row_of(name)).then_inc(vec_loaded[slot], 16)
            with sp.Fori(0, NT - 1) as i:
                sp.wait_ge(x_done, NT * NEW_X[L3B] + i + 1)
                sp.dma_start(out[bass.ds(i * P, P), :], x[:, bass.ds(i, 1), :]).then_inc(out_stored, 16)
            sp.wait_ge(x_done, NT * NEW_X[L3B] + NT)
            sp.dma_start(out[(NT - 1) * P:N, :], x[0:LAST, NT - 1, :]).then_inc(out_stored, 16)
            sp.wait_ge(out_stored, 16 * NT)

        @block.gpsimd
        def _(pool):
            nc.gpsimd.memset(ident[:, :], 0.0).then_inc(ident0, 1)
            nc.gpsimd.memset(before[:, :], 1.0).then_inc(before0, 1)
            nc.gpsimd.iota(block_lo[:, :], [[0, 1]], base=0, channel_multiplier=P,
                           allow_small_or_imprecise_dtypes=True)
            nc.gpsimd.iota(block_hi[:, :], [[0, 1]], base=P, channel_multiplier=P,
                           allow_small_or_imprecise_dtypes=True)
            nc.gpsimd.iota(unit_up[:, :].rearrange("p (u e) -> p u e", e=2), [[1, UNITS], [0, 2]], base=1,
                           channel_multiplier=0, allow_small_or_imprecise_dtypes=True)
            nc.gpsimd.iota(unit_dn[:, :].rearrange("p (u e) -> p u e", e=2), [[-1, UNITS], [0, 2]], base=UNITS,
                           channel_multiplier=0, allow_small_or_imprecise_dtypes=True)
            nc.gpsimd.iota(iota[:, :], [[1, NP]], base=0, channel_multiplier=0,
                           allow_small_or_imprecise_dtypes=True)
            pool.wait_ge(before0, 1)
            nc.gpsimd.affine_select(out=before[:, :], in_=before[:, :], compare_op=ALU.is_gt, fill=0.0, base=0,
                                    pattern=[[1, NT + 1]], channel_multiplier=-1)
            pool.wait_ge(ident0, 1)
            nc.gpsimd.affine_select(out=ident[:, :], in_=ident[:, :], compare_op=ALU.not_equal, fill=1.0,
                                    base=0, pattern=[[-1, P]], channel_multiplier=1).then_inc(pool_consts, 1)
            pool.sem_inc(c16_done, 2)
            pool.sem_inc(stage_ready, 2)

            with pool.Fori(0, NT - 1, 2) as b0:
                for par in range(2):
                    pool.wait_ge(counts_out, b0 + par + 3)
                    nc.gpsimd.tensor_copy(count16[:, bass.ds(b0 + par, 1), :],
                                          cblock[:, par, :]).then_inc(c16_done, 1)

            pool.wait_ge(cT_out, 3 * NT + 2)
            pool.wait_ge(big_ready, 1)
            big = pool.value_load(big_i[0:1, 0:1], min_val=0, max_val=1)

            def columns(s, i):
                return (countT16 if CONVS[s]["by"] == "dst" else count16)[:, :, bass.ds(i * P, P)]

            for s, c in enumerate(CONVS):
                def general_columns(i):
                    pool.wait_ge(agg_ready, tile(s, i - 1))
                    nc.gpsimd.tensor_copy(cstage[:, 0, :, :], columns(s, i)).then_inc(coarse_set, 1)
                    pool.wait_ge(coarse_set, NT * s + i + 1)
                    pool.sem_inc(passed_pool, 1)
                    with pool.Fori(0, NT) as k:
                        nc.gpsimd.tensor_copy(exact[:, :], (countT16 if c["by"] == "dst" else count16)[
                            :, bass.ds(k, 1), bass.ds(i * P, P)]).then_inc(exact_set, 1)
                        pool.wait_ge(exact_set, NT * (NT * s + i) + k + 1)
                        nc.gpsimd.tensor_tensor(cstage[:, 1, bass.ds(k, 1), :], exact[:, :].unsqueeze(1),
                                                cstage[:, 0, bass.ds(k, 1), :].bitcast(F32),
                                                ALU.subtract).then_inc(fine_set, 1)
                        pool.wait_ge(fine_set, NT * (NT * s + i) + k + 1)
                    pool.sem_inc(stage_ready, 1)

                def exact_columns(i, r):
                    pool.wait_ge(agg_ready, tile(s, i - 2))
                    nc.gpsimd.tensor_copy(cstage[:, r, :, :], columns(s, i)).then_inc(stage_ready, 1)

                def add_beta(i):
                    if s == L2:
                        pool.wait_ge(l2_w, i + 1)
                        nc.gpsimd.tensor_tensor(x[:, bass.ds(i, 1), :], x[:, bass.ds(i, 1), :],
                                                vec[:, BETA:BETA + 1, :], ALU.add).then_inc(l2_xb, 1)

                if s == L2:
                    pool.wait_ge(vec_loaded[BETA], 16)
                with pool.If(big > 0):
                    general_columns(0)
                    with pool.Fori(0, NT - 1) as i:
                        add_beta(i)
                        general_columns(i + 1)
                    add_beta(NT - 1)
                with pool.Else():
                    exact_columns(0, 0)
                    exact_columns(1, 1)
                    with pool.Fori(0, NT - 3, 2) as i0:
                        for r in range(2):
                            add_beta(i0 + r)
                            exact_columns(i0 + r + 2, r)
                    add_beta(NT - 2)
                    add_beta(NT - 1)

        @block.scalar
        def _(act):
            for s_, n in ((counts_out, 2), (cT_out, 2), (hi_done, 2), (phi_done, 2)):
                act.sem_inc(s_, n)
            act.wait_ge(dve_consts, 1)

            def split_weights(s, slot):
                for n in weights_of(s, slot):
                    _, _, _, turned, nth = weights[n]
                    if s:
                        mm_done(act, s - 1, NT - 1)
                    if not turned:
                        act.wait_ge(w_loaded, 16 * (n + 1))
                    for c in range(KF):
                        if turned:
                            act.wait_ge(wT_ready, KF * nth + c + 1)
                        nc.scalar.copy(w_hi[:, slot, c, :], ps[:, HT + c % 2, :] if turned else wstage[:, c, :]
                                       ).then_inc(whi_done, 1)

            split_weights(L0, 0)

            def turned_out(b, par):
                for g in range(3):
                    n = min(4, NT - 4 * g)
                    act.wait_ge(cT_ready, 3 * b + g + 1)
                    nc.scalar.copy(countT16[:, 4 * g:4 * g + n, bass.ds(b * P, P)],
                                   ps[:, AGG + (3 * par + g) % 2, 0:n * P].rearrange("p (n c) -> p n c", n=n)
                                   ).then_inc(cT_out, 1)

            def counts_of(b, par):
                act.wait_ge(counts_ready, b + 1)
                act.wait_ge(c16_done, b + 1)
                nc.scalar.activation(cblock[:, par, :], ps[:, 3 * par:3 * par + 3, :].rearrange("p a b -> p (a b)")[:, 0:NP],
                                     ACT.Copy, accum_out=deg_in[:, bass.ds(b, 1)]).then_inc(counts_out, 1)

            counts_of(0, 0)
            with act.Fori(1, NT - 2, 2) as b0:
                for k in range(2):
                    counts_of(b0 + k, 1 - k)
                    turned_out(b0 + k - 1, k)
            counts_of(NT - 1, 1)
            turned_out(NT - 2, 0)
            turned_out(NT - 1, 1)
            split_weights(L0, 1)

            act.wait_ge(c16_done, NT + 2)
            act.wait_ge(scale_step, 1)
            nc.scalar.activation(std[:, :], dis[:, :], ACT.Sqrt).then_inc(scale_act, 1)
            act.wait_ge(scale_act, 1)
            act.wait_ge(scale_step, 2)
            with act.Fori(0, NT) as i:
                act.wait_ge(mv_done, i + 1)
                nc.scalar.activation(std[:, bass.ds(i, 1)], mv[:, bass.ds(i, 1), 1:2], ACT.Sqrt,
                                     bias=eps[:, 0:1]).then_inc(std_done, 1)

            for s, c in enumerate(CONVS):
                def hi(i, r):
                    act.wait_ge(zT_ready, tile(s, i))
                    mm_done(act, s, i - 2)
                    nc.scalar.activation(hT_hi[:, r, :, :], ps[:, HT + r, :].rearrange("p (k n) -> p k n", k=KF),
                                         ACT.Relu).then_inc(hi_done, 1)

                def phi(i, r):
                    act.wait_ge(p_ready, tile(s, i))
                    nc.scalar.activation(p_hi[:, bass.ds(i, 1), :], ps[:, PP + r, :], ACT.Copy,
                                         scale=1.0 if c["own"] else dis[:, bass.ds(i, 1)]).then_inc(phi_done, 1)

                hi(0, 0)
                with act.Fori(0, NT - 3, 2) as i0:
                    for r in range(2):
                        hi(i0 + r + 1, 1 - r)
                        phi(i0 + r, r)
                hi(NT - 1, 1)
                phi(NT - 2, 0)
                phi(NT - 1, 1)

                if s == L0:
                    act.sem_inc(deg_out_done, 1)
                    with act.Fori(0, NT) as i:
                        act.wait_ge(deg_out_done, i + 1)
                        nc.scalar.activation(junk[:, :], countT16[:, bass.ds(i, 1), :], ACT.Copy,
                                             accum_out=deg_out[:, bass.ds(i, 1)]).then_inc(deg_out_done, 1)
                for slot, tiles in ((0, (0, 4)), (1, (4, NT))):
                    if s + 1 < len(CONVS):
                        split_weights(s + 1, slot)
                    if s + 1 in NORMED:
                        with act.Fori(*tiles) as i:
                            if s == L2:
                                act.wait_ge(l2_std, 2 * i + 1)
                                nc.scalar.activation(imv[:, 2:3], imv[:, 1:2], ACT.Sqrt,
                                                     bias=eps[:, 0:1]).then_inc(l2_std, 1)
                            act.wait_ge(mv_done, NT * NORMED[s + 1] + i + 1)
                            nc.scalar.activation(std[:, bass.ds(i, 1)], mv[:, bass.ds(i, 1), 1:2], ACT.Sqrt,
                                                 bias=eps[:, 0:1]).then_inc(std_done, 1)

        @block.vector
        def _(dve):
            for s_ in (z_ready, lo_done, plo_done, q_done, t_done):
                dve.sem_inc(s_, 2)
            nc.vector.memset(e_int[:, :, 1, :], NOWHERE).then_inc(pads_set, 1)
            nc.vector.memset(x[96:P, NT - 1, :], 0.0).then_inc(x_pad_set, 1)
            nc.vector.memset(zeros[:, :], 0.0)
            nc.vector.memset(eps[:, :], EPS).then_inc(dve_consts, 1)

            steps = [0]

            def step(ins_):
                steps[0] += 1
                ins_.then_inc(table_step, 1)
                dve.wait_ge(table_step, steps[0])

            dve.wait_ge(dst_loaded, 16 * (2 + bool(REST)))
            step(nc.vector.tensor_copy(e_f[:, 0, :, :], e_int[:, 0, :, :]))
            nc.vector.tensor_reduce(reach[:, 0:2], e_f[:, 0, :, :], AX_X, ALU.max)
            step(nc.vector.tensor_reduce(reach[:, 2:4], e_f[:, 0, :, :], AX_X, ALU.min))
            step(nc.vector.tensor_copy(reachB[:, :, :], reach[:, :].unsqueeze(2).to_broadcast([P, 4, NT])))
            dve.wait_ge(src_loaded, 16 * (2 + bool(REST)))
            step(nc.vector.tensor_copy(e_f[:, 1, :, :], e_int[:, 1, :, :]))
            dve.wait_ge(pool_consts, 1)
            dve.wait_ge(table_pe, 1)
            step(nc.vector.tensor_scalar(hit[0:NT, :], ps[0:NT, QQ, 0:ETP], block_lo[0:NT, 0:1], None, ALU.is_ge))
            step(nc.vector.scalar_tensor_tensor(hit[0:NT, :], ps[0:NT, QQ, 256:256 + ETP], block_hi[0:NT, 0:1],
                                                hit[0:NT, :], ALU.is_lt, ALU.mult))
            nc.vector.tensor_tensor(marks[0:NT, 0, :], hit[0:NT, :], unit_up[0:NT, :], ALU.mult)
            step(nc.vector.tensor_tensor(marks[0:NT, 1, :], hit[0:NT, :], unit_dn[0:NT, :], ALU.mult))
            step(nc.vector.tensor_reduce(ends[0:NT, :], marks[0:NT, :, :], AX_X, ALU.max))
            step(nc.vector.tensor_scalar(low[0:NT, :], ends[0:NT, 1:2], 1.0, -1.0, ALU.max, ALU.mult))
            step(nc.vector.scalar_tensor_tensor(length[0:NT, :], ends[0:NT, 0:1], -float(UNITS), low[0:NT, :],
                                                ALU.add, ALU.subtract))
            nc.vector.tensor_scalar(span[0:NT, 0:1], length[0:NT, :], 1.0, None, ALU.max)
            step(nc.vector.tensor_scalar(span[0:NT, 1:2], low[0:NT, :], float(UNITS), None, ALU.add))
            dve.wait_ge(table_pe, 2)
            nc.vector.tensor_copy(starts_i[0:1, 0:NT + 1], ps[0:1, QQ, 0:NT + 1])
            step(nc.vector.tensor_copy(starts[0:1, 0:NT + 1], ps[0:1, QQ, 0:NT + 1]))
            nc.vector.tensor_tensor(shift_i[0:1, 0:NT], ps[0:1, QQ, 32:32 + NT], starts[0:1, 0:NT],
                                    ALU.subtract)
            step(nc.vector.tensor_copy(nodeT[:, :, :], ps[:, QQ + 1, 0:2 * ETP].rearrange("p (k t) -> p k t", k=2)))

            def split_weights(s, slot):
                for n in weights_of(s, slot):
                    for c in range(KF):
                        dve.wait_ge(whi_done, KF * n + c + 1)
                        nc.vector.tensor_tensor(w_lo[:, slot, c, :],
                                                ps[:, HT + c % 2, :] if weights[n][3] else wstage[:, c, :],
                                                w_hi[:, slot, c, :].bitcast(F32), ALU.subtract).then_inc(wlo_done, 1)

            split_weights(L0, 0)

            def statistics(v, i):
                dve.sem_inc(passed_dve, 1)
                nc.vector.bn_stats(stats[:, :], x[:, bass.ds(i, 1), :]).then_inc(stats_done, 1)
                dve.wait_ge(stats_done, NT * v + i + 1)
                dve.sem_inc(passed_dve, 1)
                nc.vector.bn_aggr(mv_now[:, :], stats[:, :]).then_inc(aggr_done, 1)
                dve.wait_ge(aggr_done, NT * v + i + 1)
                nc.vector.tensor_scalar(mv[:, bass.ds(i, 1), :], mv_now[:, :].unsqueeze(1), 1.0, None,
                                        ALU.mult).then_inc(mv_done, 1)

            dve.wait_ge(x_loaded, 32)
            with dve.Fori(0, NT) as b:
                n0 = dve.value_load(starts_i[0:1, bass.ds(b, 1)], min_val=0, max_val=NT * UNITS)
                n1 = dve.value_load(starts_i[0:1, bass.ds(b + 1, 1)], min_val=0, max_val=NT * UNITS)
                shift = dve.value_load(shift_i[0:1, bass.ds(b, 1)])
                statistics(0, b)
                with dve.Fori(n0, n1) as n:
                    dve.wait_ge(hot_used, n + 1)
                    slot = n % RING
                    unit = dve.snap(n + shift, min_val=0, max_val=UNITS - 1)
                    for e in range(2):
                        nc.vector.tensor_scalar(src_hot[:, bass.ds(slot, 1), e, :], iota[:, :],
                                                nodeT[:, 1, bass.ds(2 * unit + e, 1)], None, ALU.is_equal)
                        last = nc.vector.tensor_scalar(dst_hot[:, bass.ds(slot, 1), e, :], iota[:, bass.ds(b * P, P)],
                                                       nodeT[:, 0, bass.ds(2 * unit + e, 1)], None, ALU.is_equal)
                    last.then_inc(hot_ready, 1)

            split_weights(L0, 1)

            dve.wait_ge(counts_out, NT + 2)
            nc.vector.tensor_reduce(top[:, :], deg_in[:, :], AX_X, ALU.max).then_inc(sem("top_done"), 1)
            nc.vector.tensor_scalar(dis[:, :], deg_in[:, :], 1.0, None, ALU.add).then_inc(scale_step, 1)
            nc.vector.tensor_scalar(inv_in[:, :], deg_in[:, :], 1.0, None, ALU.max).then_inc(sem("inv_step"), 1)
            dve.wait_ge(sem("inv_step"), 1)
            nc.vector.reciprocal(inv_in[:, :], inv_in[:, :]).then_inc(sem("inv_step"), 1)
            dve.wait_ge(scale_act, 1)
            nc.vector.reciprocal(dis[:, :], std[:, :]).then_inc(scale_step, 1)
            dve.wait_ge(scale_step, 2)
            nc.vector.tensor_tensor(dis2[:, :], dis[:, :], dis[:, :], ALU.mult).then_inc(scale_step, 1)
            dve.wait_ge(top_turned, 1)
            nc.vector.tensor_reduce(top1[:, :], ps[0:1, QQ, 0:P], AX_X, ALU.max).then_inc(sem("top_done"), 1)
            dve.wait_ge(sem("top_done"), 2)
            nc.vector.tensor_scalar(big_i[:, :], top1[:, :], EXACT, None, ALU.is_gt).then_inc(big_ready, 1)
            dve.wait_ge(c16_done, NT + 2)
            dve.wait_ge(scale_step, 3)
            dve.wait_ge(sem("inv_step"), 2)
            dve.wait_ge(big_ready, 1)

            for s, c in enumerate(CONVS):
                if s == L1A:
                    dve.wait_ge(deg_out_done, NT + 1)
                    nc.vector.tensor_scalar(has_out[:, :], deg_out[:, :], 1.0, None, ALU.min)
                    nc.vector.tensor_scalar(inv_out[:, :], deg_out[:, :], 1.0, None, ALU.max).then_inc(sem("inv_step"), 1)
                    dve.wait_ge(sem("inv_step"), 3)
                    nc.vector.reciprocal(inv_out[:, :], inv_out[:, :]).then_inc(sem("inv_step"), 1)
                    dve.wait_ge(sem("inv_step"), 4)
                scale = inv_in if s < L2 else inv_out if s == L2 else dis
                bias = vec[:, VSLOT[s], :]

                def features(i, r):
                    dve.wait_ge(zT_ready, tile(s, i - 2))
                    if c["source"] == "x":
                        n = NT * NORMED[s] + i + 1
                        dve.wait_ge(std_done, n)
                        nc.vector.reciprocal(rstd[:, bass.ds(i, 1)], std[:, bass.ds(i, 1)]).then_inc(rstd_done, 1)
                        dve.wait_ge(rstd_done, n)
                        if s:
                            dve.wait_ge(x_done, NT * NEW_X[s - 1] + i + 1)
                        nc.vector.tensor_scalar(z[:, r, :], x[:, bass.ds(i, 1), :], mv[:, bass.ds(i, 1), 0:1],
                                                rstd[:, bass.ds(i, 1)], ALU.subtract, ALU.mult).then_inc(z_ready, 1)
                    else:
                        dve.wait_ge(t_done, tile(s - 1, i))
                        nc.vector.tensor_scalar(z[:, r, :], own[:, bass.ds(i, 1), :], 1.0, None,
                                                ALU.mult).then_inc(z_ready, 1)

                def lo(i, r):
                    dve.wait_ge(hi_done, tile(s, i))
                    nc.vector.scalar_tensor_tensor(hT_lo[:, r, :, :], ps[:, HT + r, :].rearrange("p (k n) -> p k n", k=KF),
                                                   0.0, hT_hi[:, r, :, :].bitcast(F32), ALU.max,
                                                   ALU.subtract).then_inc(lo_done, 1)

                def products(i, r):
                    dve.wait_ge(phi_done, tile(s, i))
                    hi_, lo_, own_ = (t[:, bass.ds(i, 1), :] for t in (p_hi, p_lo, own))
                    if c["own"]:
                        nc.vector.tensor_tensor(lo_, ps[:, PP + r, :], hi_.bitcast(F32), ALU.subtract).then_inc(plo_done, 1)
                        dve.wait_ge(q_ready, tile(s, i))
                        if s == L2:
                            nc.vector.scalar_tensor_tensor(own_, vec[:, BNEIGH:BNEIGH + 1, :], has_out[:, bass.ds(i, 1)],
                                                           ps[:, QQ + r:QQ + r + 1, :], ALU.mult, ALU.add).then_inc(q_half, 1)
                            dve.wait_ge(q_half, i + 1)
                            nc.vector.tensor_tensor(own_, own_, bias.unsqueeze(1), ALU.add).then_inc(q_done, 1)
                        else:
                            nc.vector.tensor_tensor(own_, ps[:, QQ + r, :], bias, ALU.add).then_inc(q_done, 1)
                    else:
                        nc.vector.scalar_tensor_tensor(lo_, ps[:, PP + r, :], dis[:, bass.ds(i, 1)], hi_.bitcast(F32),
                                                       ALU.mult, ALU.subtract).then_inc(plo_done, 1)
                        nc.vector.scalar_tensor_tensor(own_, ps[:, PP + r, :], dis2[:, bass.ds(i, 1)], bias,
                                                       ALU.mult, ALU.add).then_inc(q_done, 1)

                features(0, 0)
                features(1, 1)
                lo(0, 0)
                dve.wait_ge(vec_loaded[VSLOT[s]], VCOUNT[s])
                if s == L2:
                    dve.wait_ge(vec_loaded[BNEIGH], 16)
                with dve.Fori(0, NT - 3, 2) as i0:
                    for r in range(2):
                        features(i0 + r + 2, r)
                        lo(i0 + r + 1, 1 - r)
                        products(i0 + r, r)
                lo(NT - 1, 1)
                products(NT - 2, 0)
                products(NT - 1, 1)

                def combine(i, r):
                    dve.wait_ge(agg_ready, tile(s, i))
                    dve.wait_ge(q_done, tile(s, i))
                    x_, own_ = x[:, bass.ds(i, 1), :], own[:, bass.ds(i, 1), :]
                    mixed = own_
                    nc.vector.scalar_tensor_tensor(mixed, ps[:, AGG + r:AGG + r + 1, :], scale[:, bass.ds(i, 1)], own_,
                                                   ALU.mult, ALU.add).then_inc(t_done, 1)
                    if s not in NEW_X:
                        return
                    dve.wait_ge(t_done, tile(s, i))
                    if s == L0:
                        nc.vector.scalar_tensor_tensor(x_, mixed, 0.0, x_, ALU.max, ALU.add).then_inc(x_done, 1)
                    elif s == L2:
                        n = [0]

                        def link(ins_):
                            n[0] += 1
                            ins_.then_inc(l2_step, 1)
                            dve.wait_ge(l2_step, L2_STEPS * i + n[0])

                        z2 = mix2[:, :].unsqueeze(1)
                        nc.vector.tensor_scalar(mixed, mixed, 0.0, None, ALU.max)
                        link(nc.vector.tensor_scalar(z2, x_, mv[:, bass.ds(i, 1), 0:1], rstd[:, bass.ds(i, 1)],
                                                     ALU.subtract, ALU.mult))
                        link(nc.vector.scalar_tensor_tensor(z2, z2, 0.0, mixed, ALU.max, ALU.add))
                        dve.sem_inc(l2_w, 1)
                        link(nc.vector.bn_stats(stats[:, :], z2))
                        dve.sem_inc(passed_dve, 1)
                        nc.vector.bn_aggr(imv[:, 0:2], stats[:, :]).then_inc(l2_std, 1)
                        dve.wait_ge(l2_std, 2 * i + 2)
                        link(nc.vector.reciprocal(imv[:, 3:4], imv[:, 2:3]))
                        link(nc.vector.tensor_scalar(z2, z2, imv[:, 0:1], imv[:, 3:4], ALU.subtract, ALU.mult))
                        link(nc.vector.tensor_tensor(z2, z2, vec[:, GAMMA:GAMMA + 1, :], ALU.mult))
                        assert n[0] == L2_STEPS
                        dve.wait_ge(l2_xb, i + 1)
                        nc.vector.tensor_tensor(x_, x_, z2, ALU.add).then_inc(x_done, 1)
                    else:
                        nc.vector.tensor_tensor(x_, x_, mixed, ALU.add).then_inc(x_done, 1)
                    if s + 1 in NORMED:
                        dve.wait_ge(x_done, NT * NEW_X[s] + i + 1)
                        statistics(NORMED[s + 1], i)

                L2_STEPS = 6
                if s == L2:
                    dve.wait_ge(vec_loaded[GAMMA], 16)
                for slot, tiles in ((0, (0, 3, 2)), (1, (4, NT - 1, 2))):
                    if s + 1 < len(CONVS):
                        split_weights(s + 1, slot)
                    with dve.Fori(*tiles) as i0:
                        for r in range(2):
                            combine(i0 + r, r)

        @block.tensor
        def _(pe):
            pe.sem_inc(hot_used, RING)
            for s_ in (zT_ready, p_ready, q_ready, agg_ready):
                pe.sem_inc(s_, 2)

            pe.wait_ge(pool_consts, 1)
            pe.wait_ge(table_step, 3)
            for k in range(4):
                last = nc.tensor.transpose(ps[0:NT, QQ, k * P:(k + 1) * P], reachB[:, k, :], ident[:, :])
            last.then_inc(table_pe, 1)
            pe.wait_ge(table_step, 4)
            for k in range(2):
                nc.tensor.transpose(ps[:, QQ + 1, k * ETP:k * ETP + P], e_f[:, k, 0, :], ident[:, :])
                nc.tensor.transpose(ps[:, QQ + 1, k * ETP + P:(k + 1) * ETP], e_f[0:ETP - P, k, 1, :],
                                    ident[0:ETP - P, 0:ETP - P])
            pe.wait_ge(table_step, 11)
            nc.tensor.matmul(ps[0:1, QQ, 0:NT + 1], span[0:NT, 0:1], before[0:NT, :], start=True, stop=True)
            nc.tensor.matmul(ps[0:1, QQ, 32:32 + NT], span[0:NT, 1:2], ident[0:NT, 0:NT], start=True,
                             stop=True).then_inc(table_pe, 1)

            def turn_weights(s, slot):
                for n in weights_of(s, slot):
                    if not weights[n][3]:
                        continue
                    pe.wait_ge(w_loaded, 16 * (n + 1))
                    if s:
                        pe.wait_ge(lo_done, tile(s - 1, NT - 1))
                    for c in range(KF):
                        if KF * n + c >= 2:
                            pe.wait_ge(wlo_done, KF * n + c - 1)
                        for o in range(KF):
                            last = nc.tensor.transpose(ps[:, HT + c % 2, o * P:(o + 1) * P],
                                                       wstage[:, o, c * P:(c + 1) * P], ident[:, :])
                        last.then_inc(wT_ready, 1)

            turn_weights(L0, 0)

            cuts = [(a, min(a + 512, NP)) for a in range(0, NP, 512)]

            def count(b, par):
                n0 = pe.value_load(starts_i[0:1, bass.ds(b, 1)], min_val=0, max_val=NT * UNITS)
                n1 = pe.value_load(starts_i[0:1, bass.ds(b + 1, 1)], min_val=0, max_val=NT * UNITS)
                pe.wait_ge(counts_out, b + 1)
                for k, (a, e_) in enumerate(cuts):
                    nc.tensor.matmul(ps[:, 3 * par + k, 0:e_ - a], zeros[:, 0:P], zeros[:, 0:e_ - a],
                                     start=True, stop=False)
                with pe.Fori(n0, n1) as n:
                    pe.wait_ge(hot_ready, n + 1)
                    slot = n % RING
                    for e in range(2):
                        for k, (a, e_) in enumerate(cuts):
                            last = nc.tensor.matmul(ps[:, 3 * par + k, 0:e_ - a], dst_hot[:, bass.ds(slot, 1), e, :],
                                                    src_hot[:, bass.ds(slot, 1), e, a:e_], start=False, stop=False)
                    last.then_inc(hot_used, 1)
                for k, (a, e_) in enumerate(cuts):
                    last = nc.tensor.matmul(ps[:, 3 * par + k, 0:e_ - a], zeros[:, 0:P], zeros[:, 0:e_ - a],
                                            start=False, stop=True)
                last.then_inc(counts_ready, 1)

            def turn_counts(b, par):
                pe.wait_ge(counts_out, b + 3)
                for g in range(3):
                    pe.wait_ge(cT_out, 3 * b + g + 1)
                    for j in range(4 * g, min(4 * g + 4, NT)):
                        last = nc.tensor.transpose(ps[:, AGG + (3 * par + g) % 2, (j - 4 * g) * P:(j - 4 * g + 1) * P],
                                                   cblock[:, par, j * P:(j + 1) * P], ident[:, :])
                    last.then_inc(cT_ready, 1)

            pe.wait_ge(dve_consts, 1)
            pe.wait_ge(table_step, steps_of_table)
            pe.wait_ge(wlo_done, KF)
            count(0, 0)
            with pe.Fori(1, NT - 2, 2) as b0:
                for k in range(2):
                    count(b0 + k, 1 - k)
                    turn_counts(b0 + k - 1, k)
            count(NT - 1, 1)
            turn_counts(NT - 2, 0)
            turn_counts(NT - 1, 1)
            turn_weights(L0, 1)
            pe.wait_ge(sem("top_done"), 1)
            nc.tensor.transpose(ps[0:1, QQ, 0:P], top[:, 0:1], ident[:, :]).then_inc(top_turned, 1)
            pe.wait_ge(big_ready, 1)
            big = pe.value_load(big_i[0:1, 0:1], min_val=0, max_val=1)

            for s, c in enumerate(CONVS):
                def turn(i, r):
                    pe.wait_ge(z_ready, tile(s, i))
                    pe.wait_ge(lo_done, tile(s, i - 2))
                    for k in range(KF):
                        last = nc.tensor.transpose(ps[:, HT + r, k * P:(k + 1) * P], z[:, r, k * P:(k + 1) * P], ident[:, :])
                    last.then_inc(zT_ready, 1)

                def times(bank, r, slot):
                    pairs = [(a, w, k) for k in range(KF) for a, w in ((hT_hi, w_hi), (hT_hi, w_lo), (hT_lo, w_hi))]
                    for n, (a, w, k) in enumerate(pairs):
                        last = nc.tensor.matmul(ps[:, bank + r, :], a[:, r, k, :], w[:, slot, k, :],
                                                start=n == 0, stop=n == len(pairs) - 1)
                    return last

                def products(i, r):
                    pe.wait_ge(lo_done, tile(s, i))
                    pe.wait_ge(plo_done if c["own"] else q_done, tile(s, i - 2))
                    times(PP, r, 0).then_inc(p_ready, 1)
                    if c["own"]:
                        pe.wait_ge(q_done, tile(s, i - 2))
                        times(QQ, r, 1).then_inc(q_ready, 1)

                pe.wait_ge(wlo_done, KF * (weights_of(s)[-1] + 1))
                turn(0, 0)
                with pe.Fori(0, NT - 3, 2) as i0:
                    for r in range(2):
                        turn(i0 + r + 1, 1 - r)
                        products(i0 + r, r)
                turn(NT - 1, 1)
                products(NT - 2, 0)
                products(NT - 1, 1)

                def aggregate(i, r, parts):
                    pe.wait_ge(stage_ready, tile(s, i))
                    pe.wait_ge(t_done, tile(s, i - 2))
                    pe.wait_ge(plo_done, tile(s, NT - 2))
                    n = 0
                    for k in range(NT):
                        if k == NT - 1:
                            pe.wait_ge(plo_done, tile(s, NT - 1))
                        for part in parts:
                            for p_ in (p_hi, p_lo):
                                n += 1
                                last = nc.tensor.matmul(ps[:, AGG + r, :], cstage[:, part, k, :], p_[:, k, :],
                                                        start=n == 1, stop=n == 2 * len(parts) * NT)
                    last.then_inc(agg_ready, 1)

                for slot, tiles in ((0, (0, 3, 2)), (1, (4, NT - 1, 2))):
                    if s + 1 < len(CONVS):
                        turn_weights(s + 1, slot)
                    with pe.If(big > 0):
                        with pe.Fori(*tiles) as i0:
                            for r in range(2):
                                aggregate(i0 + r, r, (0, 1))
                    with pe.Else():
                        with pe.Fori(*tiles) as i0:
                            for r in range(2):
                                aggregate(i0 + r, r, (r,))


steps_of_table = 13

_INS = ["x", "src", "dst", "L0_gnn_W_l", "L0_gnn_b_l", "L0_gnn_W_r", "L1_gnn_W1l", "L1_gnn_b1", "L1_gnn_W1r",
        "L1_gnn_W2l", "L1_gnn_b2", "L1_gnn_W2r", "L2_gnn_W_self", "L2_gnn_b_self", "L2_gnn_W_neigh", "L2_gnn_b_neigh",
        "L2_gnn_ln_gamma", "L2_gnn_ln_beta", "L3_gnn_W1", "L3_gnn_b1", "L3_gnn_W2", "L3_gnn_b2"]


def kernel(**inputs):
    import numpy as _np
    import concourse.bacc as _bacc
    from concourse.bass_utils import run_bass_kernel_spmd as _run

    nc = _bacc.Bacc("TRN2", target_bir_lowering=False, num_devices=1)
    arrays, args = {}, {}
    for name in _INS:
        a = _np.ascontiguousarray(inputs[name])
        arrays[f"in_{name}"] = a
        args[name] = nc.dram_tensor(f"in_{name}", a.shape, mybir.dt.from_np(a.dtype), kind="ExternalInput").ap()
    shape = inputs["x"].shape
    out = nc.dram_tensor("out_x", shape, F32, kind="ExternalOutput").ap()
    gnn_kernel(nc, args, out)
    r = _run(nc, [arrays], core_ids=[0])
    return r.results[0]["out_x"]
```
